# Optimizing a Trainium2 kernel written in Bass

```python
import numpy as np
import jax
import jax.numpy as jnp

def _softmax(x, axis=-1):
    return jax.nn.softmax(x, axis=axis)
def _gelu(x):
    return jax.nn.gelu(x, approximate=True)
def _silu(x):
    return jax.nn.silu(x)
def _sigmoid(x):
    return jax.nn.sigmoid(x)
def _layernorm(x, axis=-1, eps=1e-5):
    m = jnp.mean(x, axis=axis, keepdims=True)
    v = jnp.var(x, axis=axis, keepdims=True)
    return (x - m) / jnp.sqrt(v + eps)
def _scatter_add(tgt, idx, src, axis=0):
    return tgt.at[idx].add(src)
def _segment_sum(src, seg, n):
    return jax.ops.segment_sum(src, seg, n)

kernel_name = 'mk_metaformer_d1_conv_nchw128_661d36'

def setup_inputs(seed: int = 0):
    np.random.seed(seed)
    _w = jnp.asarray
    def _rec_inputs():
        import jax
        import jax.numpy as jnp
        _gk = jax.random.key(seed)
        x = 7.22e-05 + 1 * jax.random.normal(jax.random.fold_in(_gk, 1), (16, 128, 64, 64), jnp.float32)
        return x
    x = _rec_inputs()
    def _L0_conv_setup():
        import jax, jax.numpy as jnp
        import numpy as np
        from jax import lax
        DN = ('NCHW', 'OIHW', 'NCHW')
        key = jax.random.key(seed)
        k1, k2, k3 = jax.random.split(key, 3)
        B, C, H, W = (16, 128, 64, 64)
        hid, ker = (128, 3)
        x = jax.random.normal(k1, (B, C, H, W), dtype=jnp.float32)
        W_is = jax.random.normal(k2, (4 * hid, C, 1, ker), dtype=jnp.float32) * 0.02
        b_is = jnp.zeros((4 * hid,), dtype=jnp.float32)
        W_ss = jax.random.normal(k3, (4 * hid, hid, 1, ker), dtype=jnp.float32) * 0.02
        b_ss = jnp.zeros((4 * hid,), dtype=jnp.float32)
        return {'x': x, 'W_is': W_is, 'b_is': b_is, 'W_ss': W_ss, 'b_ss': b_ss}
    _L0_conv_all = _L0_conv_setup()
    _L0_conv_in = {k: v for k, v in _L0_conv_all.items() if k in ('W_is', 'b_is', 'W_ss', 'b_ss', )}
    del _L0_conv_all

    def _L0_ffn_setup():
        import jax, jax.numpy as jnp
        import numpy as np
        BN_EPS = 1e-05
        key = jax.random.key(seed)
        k1, k2, k3 = jax.random.split(key, 3)
        B, T, I, H = (64, 2048, 128, 128)
        x = jax.random.normal(k1, (B, T, I), dtype=jnp.float32)
        W = jax.random.normal(k2, (H, I), dtype=jnp.float32) * (1.0 / np.sqrt(I))
        V = jnp.linalg.qr(jax.random.normal(k3, (H, H), dtype=jnp.float32))[0]
        gamma = jnp.ones((H,), dtype=jnp.float32)
        beta = jnp.zeros((H,), dtype=jnp.float32)
        return {'x': x, 'W': W, 'V': V, 'gamma': gamma, 'beta': beta}
    _L0_ffn_all = _L0_ffn_setup()
    _L0_ffn_in = {k: v for k, v in _L0_ffn_all.items() if k in ('W', 'V', 'gamma', 'beta', )}
    del _L0_ffn_all

    return {
        "x": x,
        "L0_conv_W_is": _L0_conv_in["W_is"],
        "L0_conv_b_is": _L0_conv_in["b_is"],
        "L0_conv_W_ss": _L0_conv_in["W_ss"],
        "L0_conv_b_ss": _L0_conv_in["b_ss"],
        "L0_ffn_W": _L0_ffn_in["W"],
        "L0_ffn_V": _L0_ffn_in["V"],
        "L0_ffn_gamma": _L0_ffn_in["gamma"],
        "L0_ffn_beta": _L0_ffn_in["beta"],
    }

def reference(x, L0_conv_W_is, L0_conv_b_is, L0_conv_W_ss, L0_conv_b_ss, L0_ffn_W, L0_ffn_V, L0_ffn_gamma, L0_ffn_beta):
    import jax
    import jax.numpy as jnp
    def _L0_conv_ref(x, W_is, b_is, W_ss, b_ss):
        import jax, jax.numpy as jnp
        import numpy as np
        from jax import lax
        DN = ('NCHW', 'OIHW', 'NCHW')
        B, C, H, W = x.shape
        hid = W_ss.shape[1]
        ker = W_is.shape[-1]
        pad = ker // 2
        col_mask = (jnp.arange(ker) <= pad).astype(x.dtype)
        Wm = W_is * col_mask
        z_is = lax.conv_general_dilated(x, Wm, (1, 1), [(0, 0), (pad, pad)], dimension_numbers=DN) + b_is[None, :, None, None]
        h0 = jnp.zeros((B, hid, W), dtype=x.dtype)
        c0 = jnp.zeros((B, hid, W), dtype=x.dtype)

        def step(carry, z_row):
            h, c = carry
            z_ss = lax.conv_general_dilated(h[:, :, None, :], W_ss, (1, 1), [(0, 0), (pad, pad)], dimension_numbers=DN)[:, :, 0, :]
            z = z_row + z_ss + b_ss[None, :, None]
            i_g = jax.nn.sigmoid(z[:, 0 * hid:1 * hid])
            f_g = jax.nn.sigmoid(z[:, 1 * hid:2 * hid])
            o_g = jax.nn.sigmoid(z[:, 2 * hid:3 * hid])
            g = jnp.tanh(z[:, 3 * hid:4 * hid])
            c = f_g * c + i_g * g
            h = o_g * jnp.tanh(c)
            return ((h, c), h)
        z_rows = jnp.moveaxis(z_is, 2, 0)
        _, outs = lax.scan(step, (h0, c0), z_rows)
        return jnp.moveaxis(outs, 0, 2)

    def _L0_ffn_ref(x, W, V, gamma, beta):
        import jax, jax.numpy as jnp
        import numpy as np
        BN_EPS = 1e-05
        B, T, H = (x.shape[0], x.shape[1], W.shape[0])
        Wx = jnp.einsum('bti,hi->bth', x, W)
        flat = Wx.reshape(B * T, H)
        mean = jnp.mean(flat, axis=0)
        var = jnp.var(flat, axis=0)
        Wx = ((flat - mean) * jax.lax.rsqrt(var + BN_EPS) * gamma + beta).reshape(B, T, H)
        Vt = V.T

        def step(yt, wx_t):
            yt = jax.nn.sigmoid(wx_t + yt @ Vt)
            return (yt, yt)
        y0 = jnp.zeros((B, H), dtype=Wx.dtype)
        _, ys = jax.lax.scan(step, y0, jnp.swapaxes(Wx, 0, 1))
        return jnp.swapaxes(ys, 0, 1)

    def _gn(v, G=32, eps=1e-5):
        B_, C_, H_, W_ = v.shape
        g = v.reshape(B_, G, C_ // G, H_, W_)
        m = jnp.mean(g, axis=(2, 3, 4), keepdims=True)
        s = jnp.var(g, axis=(2, 3, 4), keepdims=True)
        return ((g - m) / jnp.sqrt(s + eps)).reshape(v.shape)

    def _ln_c(v, eps=1e-6):
        m = jnp.mean(v, axis=1, keepdims=True)
        s = jnp.var(v, axis=1, keepdims=True)
        return (v - m) / jnp.sqrt(s + eps)

    def _ln_t(v, eps=1e-5):
        m = jnp.mean(v, axis=-1, keepdims=True)
        s = jnp.var(v, axis=-1, keepdims=True)
        return (v - m) / jnp.sqrt(s + eps)

    def _to_tokens(v):
        B_, C_, H_, W_ = v.shape
        return v.reshape(B_, C_, H_ * W_).transpose(0, 2, 1)
    def _from_tokens(t, like):
        B_, C_, H_, W_ = like.shape
        return t.transpose(0, 2, 1).reshape(B_, C_, H_, W_)

    x = x + _L0_conv_ref(_ln_c(x), L0_conv_W_is, L0_conv_b_is, L0_conv_W_ss, L0_conv_b_ss)
    t = _to_tokens(x)
    t = t + _L0_ffn_ref(_ln_t(t), L0_ffn_W, L0_ffn_V, L0_ffn_gamma, L0_ffn_beta)
    x = _from_tokens(t, x)
    return x


_drawn_inputs = setup_inputs


def setup_inputs(seed=0):
    import zlib

    import numpy as np

    out = dict(_drawn_inputs(seed))
    spreads = {'L0_conv_b_is': (0.0, 0.1),
     'L0_conv_b_ss': (0.0, 0.1),
     'L0_ffn_gamma': (1.0, 0.551),
     'L0_ffn_beta': (0.0, 0.41)}
    factors = {'L0_conv_W_ss': 4.143}
    for name, (base, spread) in spreads.items():
        noise = np.random.default_rng([zlib.crc32(name.encode()), seed]).standard_normal(out[name].shape)
        drawn = base * np.exp(spread * noise) if base else spread * noise
        out[name] = jnp.asarray(drawn.astype(out[name].dtype))
    for name, factor in factors.items():
        out[name] = (out[name] * factor).astype(out[name].dtype)
    return out
```

```python
from contextlib import ExitStack

import concourse.bass as bass
from concourse import mybir

F32, F16, BF16 = mybir.dt.float32, mybir.dt.float16, mybir.dt.bfloat16
I32 = mybir.dt.int32
ALU = mybir.AluOpType
ACT = mybir.ActivationFunctionType
AX = mybir.AxisListType

B, C, H, W = 16, 128, 64, 64
G = 2
GB = B // G
N = GB * W
ROW = B * W
GATE_ROWS = (3, 0, 1, 2)
XT, HT = 2, 3
TAPS = XT + HT
SW = 8
SLICES = W // SW
SC = B * SW
RING, FIRST_KEPT = 3, 5
SLOT = H * SC
Q = 4
QH = H // Q
QC = QH * B
WARM = 12
CONV_EPS, TOKEN_EPS, BN_EPS = 1e-6, 1e-5, 1e-5
OPERAND_SCALE = 2.0 ** 11
WEIGHT_SCALE = 2.0 ** 14
TOLERANCE = 2.0 ** -22
COMPARED = (H - 1) * B


def slot_of(ws):
    return ws % RING + RING * (ws // FIRST_KEPT)


class Row:

    def __init__(self, i, off):
        self.i, self.off, self.p = i, off, off % 2

    def __add__(self, d):
        return Row(self.i, self.off + d)

    def count(self, per_row, more=0):
        return self.i * (2 * per_row) + (per_row * self.off + more)

    def pair(self, each, more=0):
        return self.i * each + (each * (self.off // 2) + more)


def build(nc, x_d, wis_d, wss_d, bis_d, bss_d, wf_d, v_d, gamma_d, beta_d, out_d, force_exact=False):
    x1_d = nc.dram_tensor("x1_scratch", (C, SLICES, H, SC), F32, kind="Internal").ap()
    wx_d = nc.dram_tensor("wx_scratch", (C, SLICES, H, SC), F32, kind="Internal").ap()
    ctx = ExitStack()
    with ctx:
        def sem(name):
            return ctx.enter_context(nc.semaphore(name))

        slices = ctx.enter_context(nc.sbuf_tensor("slices", [C, 2 * RING * SLOT], F32))
        extra = ctx.enter_context(nc.sbuf_tensor("extra", [C, 3968], F32))
        taken = {"slices": 0, "extra": 0}

        def carve(size, dt=F32, of="slices"):
            words = size if dt in (F32, I32) else (size + 1) // 2
            words += words % 2
            a = taken[of]
            taken[of] = a + words
            assert taken[of] <= (RING * SLOT if of == "slices" else 3968), (of, taken)
            v = (slices if of == "slices" else extra)[:, a:a + words]
            return v if dt == F32 else v.bitcast(dt)[:, 0:size]

        x_ring = carve(4 * ROW).rearrange("c (r n) -> c r n", r=4)
        x1 = [carve(ROW) for _ in range(2)]
        split = {ln: (carve(ROW, BF16), carve(ROW, BF16)) for ln in (1, 2)}
        d = {ln: carve(ROW) for ln in (1, 2)}
        sq = {ln: carve(ROW) for ln in (1, 2)}
        rs = {ln: carve(ROW) for ln in (1, 2)}
        xn = [[carve(B * (W + 1), F16).rearrange("c (b w) -> c b w", b=B) for _ in range(2)] for _ in range(2)]
        yn = [carve(ROW, F16) for _ in range(2)]
        hs = [carve(B * (W + 2), F16).rearrange("c (b w) -> c b w", b=B) for _ in range(2)]
        stage = [carve(ROW) for _ in range(2)]
        wc = [carve(TAPS * 4 * C, F16).rearrange("c (k g o) -> c k g o", k=TAPS, g=4) for _ in range(2)]
        wf = [carve(C, F16, "extra") for _ in range(2)]
        ones_bf = carve(C, BF16, "extra")
        bn_parts = carve(H * 2 * 6, F32, "extra").rearrange("c (r s) -> c r s", s=6)
        v_sb = carve(C, F32, "extra")
        small = carve(64, F32, "extra")
        raw = slices[:, RING * SLOT:RING * SLOT + (TAPS * 4 + 1) * C]
        raw_c = raw[:, 0:TAPS * 4 * C].rearrange("c (k g o) -> c k g o", k=TAPS, g=4)
        raw_f = raw[:, TAPS * 4 * C:]
        ones_f = carve(C, F32, "extra")
        cells = carve(5 * N, F32, "extra")
        cell = [cells[:, g * N:(g + 1) * N] for g in range(G)]
        gg = cells[:, 2 * N:3 * N]
        hh = [cells[:, (3 + g) * N:(4 + g) * N] for g in range(G)]
        warm_y = [cells[:, j * ROW:(j + 1) * ROW] for j in range(2)]

        bias_is, bias_ss, bias = small[:, 0:4], small[:, 4:8], small[:, 8:12]
        gamma, beta = small[:, 12:13], small[:, 13:14]
        most, least = small[:, 14:19], small[:, 20:25]
        most_all, least_all = small[:, 26:31], small[:, 32:37]
        unscale, rescale = small[:, 38:43], small[:, 44:49]
        eps = {1: small[:, 50:51], 2: small[:, 51:52]}
        bn, bn_s, bn_b, half = small[:, 52:54], small[:, 54:55], small[:, 55:56], small[:, 56:57]
        same, flag = small[:, 57:58], small[:, 58:59].bitcast(I32)
        bn_t = small[:, 59:60]

        gate_ps = [ctx.enter_context(nc.psum_tensor(f"gate_ps{k}", [C, N], F32)) for k in range(4)]
        p_ps = ctx.enter_context(nc.psum_tensor("p_ps", [C, ROW], F32))
        q_ps = ctx.enter_context(nc.psum_tensor("q_ps", [C, ROW], F32))
        mean_ps, var_ps = {1: p_ps, 2: p_ps}, {1: q_ps, 2: p_ps}

        loaded, ready0 = sem("loaded"), sem("ready0")
        prep, prep_pool = sem("prep"), sem("prep_pool")
        x_in = [sem(f"x_in{p}") for p in range(2)]
        x1_out = [sem(f"x1_out{p}") for p in range(2)]
        wx_out = [sem(f"wx_out{p}") for p in range(2)]
        hi_done, lo_done, mean_done, d_done, sqhi_done, sqlo_done, var_done, ln_done, exp_done, rsq_done, u_done, w_done, \
            norm_done, nhi_done, nlo_done = (
                {ln: sem(f"{name}{ln}") for ln in (1, 2)} for name in (
                    "hi", "lo", "mean", "d", "sqhi", "sqlo", "var", "ln", "exp", "rsq", "u", "w", "norm", "nhi", "nlo"))
        gate_done, g_done, i_done, f_done, o_done, tc_done = (sem(s) for s in ("gate", "g", "i", "f", "o", "tc"))
        ig_done, fc_done, c_done, h_done, hhi_done, hlo_done, x1_done = (
            sem(s) for s in ("ig", "fc", "c", "h", "hhi", "hlo", "x1"))
        ffn_done, ev_done, bn_done = sem("ffn"), sem("ev"), sem("bn_part")
        bn_step, bn_ready = sem("bn_step"), sem("bn_ready")
        slice_in = sem("slice_in")
        slice_out = [sem(f"slice_out{ws}") for ws in range(SLICES)]
        vy_done, z_done, y_done = ([sem(f"{s}{q}") for q in range(Q)] for s in ("vy", "z", "y"))
        cmp_step, cmp_sum, flag_ready = sem("cmp_step"), sem("cmp_sum"), sem("flag_ready")
        ex_in, ex_out, ex_vy, ex_z, ex_y, ex_add = (sem(s) for s in ("ex_in", "ex_out", "ex_vy", "ex_z", "ex_y", "ex_add"))

        ex_wx = slices[:, 0:ROW].rearrange("c (s n) -> c s n", s=SLICES)
        ex_x1 = slices[:, ROW:2 * ROW].rearrange("c (s n) -> c s n", s=SLICES)
        ex_state = cells[:, 4 * N:4 * N + B]

        block = ctx.enter_context(nc.Block())

        LOADS = 8
        PREP = 11

        def rows(engine, row):
            def one(t):
                row(Row(t // 2, t % 2), ln1=t + 2 < H, fin1=0 <= t + 1 < H, gates=0 <= t < H, ln2=0 <= t - 1 < H,
                    ffn=0 <= t - 2 < H, t=t)
            for t in range(-2, 4):
                one(t)
            with engine.Fori(2, (H - 4) // 2) as i:
                for p in range(2):
                    row(Row(i, p), ln1=True, fin1=True, gates=True, ln2=True, ffn=True, t=None)
            for t in range(H - 4, H + 2):
                one(t)

        def slot4(row):
            return row.count(1) % 4

        def group(v, g):
            return v[:, g * N:(g + 1) * N].rearrange("c (b w) -> c b w", b=GB)

        def columns(at, q, w):
            return slices[:, bass.ds(at + (q * QC * SW + w), QC, step=SW)]

        def warm_columns(tile, q):
            return tile[:, B if q == 0 else q * QC:(q + 1) * QC]

        def warm_source(j, q):
            w = W - WARM + j
            first = (q * QH - 1) * SC if q else 0
            n = QC - (0 if q else B)
            a = slot_of(w // SW) * SLOT + first + w % SW
            return slices[:, bass.ds(a, n, step=SW)]

        @block.sync
        def _(sp):
            for dst, src in ((raw_c[:, 0:XT], wis_d), (raw_c[:, XT:TAPS], wss_d), (raw_f, wf_d), (v_sb, v_d),
                             (bias_is, bis_d), (bias_ss, bss_d), (gamma, gamma_d), (beta, beta_d)):
                sp.dma_start(dst, src).then_inc(loaded, 16)

            def load_x(r, t):
                if t is None or t >= 4:
                    sp.wait_ge(x1_done, r.count(2, -6))
                elif t >= 2:
                    sp.wait_ge(x_in[r.p], r.pair(16))
                sp.dma_start(x_ring[:, bass.ds(slot4(r), 1), :], x_d[:, bass.ds(r.count(1), 1), :]).then_inc(x_in[r.p], 16)

            load_x(Row(0, 0), 0)

            def row(r, ln1, fin1, gates, ln2, ffn, t):
                if t is None or t + 3 < H:
                    load_x(r + 3, None if t is None else t + 3)
                if ln2:
                    r1 = r + -1
                    sp.wait_ge(x1_done, r1.count(2, 2))
                    src = x1[r1.p].rearrange("c (s n) -> c s n", s=SLICES)
                    for dst in (out_d, x1_d):
                        sp.dma_start(dst[:, :, bass.ds(r1.count(1), 1), :].rearrange("c s r n -> c s (r n)"),
                                     src).then_inc(x1_out[r1.p], 16)
                if ffn:
                    r2 = r + -2
                    sp.wait_ge(ev_done, r2.count(1, 1))
                    src = stage[r2.p].rearrange("c (s n) -> c s n", s=SLICES)
                    sp.dma_start(wx_d[:, :, bass.ds(r2.count(1), 1), :].rearrange("c s r n -> c s (r n)"),
                                 src).then_inc(wx_out[r2.p], 16)
                    kept = slices[:, :].rearrange("c (k h n) -> c k h n", k=2 * RING, h=H)
                    for a, b in ((FIRST_KEPT, FIRST_KEPT + 1), (FIRST_KEPT + 1, SLICES)):
                        s = slot_of(a)
                        sp.dma_start(kept[:, s:s + b - a, bass.ds(r2.count(1), 1), :].rearrange("c s r n -> c s (r n)"),
                                     src[:, a:b, :]).then_inc(wx_out[r2.p], 16)

            rows(sp, row)
            for p in range(2):
                sp.wait_ge(wx_out[p], 48 * H // 2)
                sp.wait_ge(x1_out[p], 32 * H // 2)
            sp.wait_ge(bn_done, H)
            for ws in range(FIRST_KEPT):
                s = slot_of(ws)
                if ws:
                    sp.wait_ge(slice_in, 16 * ws)
                if ws >= RING:
                    sp.wait_ge(slice_out[ws - RING], 16)
                    for q in range(Q):
                        sp.wait_ge(vy_done[q], WARM + (ws - RING + 1) * SW)
                sp.dma_start(slices[:, s * SLOT:(s + 1) * SLOT],
                             wx_d[:, ws, :, :].rearrange("c h n -> c (h n)")).then_inc(slice_in, 16)
            for ws in range(SLICES):
                sp.wait_ge(slice_out[ws], 16)
            sp.wait_ge(flag_ready, 1)
            f = sp.value_load(flag[0:1, 0:1])
            with sp.If(f < 1):
                with sp.Fori(0, H) as h:
                    sp.wait_ge(ex_out, h * 16)
                    sp.dma_start(ex_wx, wx_d[:, :, bass.ds(h, 1), :].rearrange("c s r n -> c s (r n)")).then_inc(ex_in, 16)
                    sp.dma_start(ex_x1, x1_d[:, :, bass.ds(h, 1), :].rearrange("c s r n -> c s (r n)")).then_inc(ex_in, 16)
                    sp.wait_ge(ex_add, h * W + W)
                    sp.dma_start(out_d[:, :, bass.ds(h, 1), :].rearrange("c s r n -> c s (r n)"), ex_x1).then_inc(ex_out, 16)
                sp.wait_ge(ex_out, 16 * H)
            sp.nop()

        @block.tensor
        def _(pe):
            pe.wait_ge(ready0, 1)

            def passes(out, parts):
                last = None
                for n, (w, v) in enumerate(parts):
                    last = nc.tensor.matmul(out, w, v, start=(n == 0), stop=(n == len(parts) - 1))
                return last

            def sums(ps, ln, done):
                hi, lo = split[ln]
                for b in range(2):
                    c = slice(b * N, (b + 1) * N)
                    last = passes(ps[:, c], [(ones_bf, hi[:, c]), (ones_bf, lo[:, c])])
                last.then_inc(done[ln], 1)

            def gate(r, g, k, t):
                if t != 0 or g:
                    pe.wait_ge((g_done, ig_done, fc_done, h_done)[k], r.count(2, g))
                bs = slice(g * GB, (g + 1) * GB)
                row = GATE_ROWS[k]
                parts = []
                for tap in range(XT):
                    hi, lo = (xn[r.p][j][:, bs, tap:tap + W] for j in range(2))
                    parts += [(wc[0][:, tap, row], hi), (wc[0][:, tap, row], lo), (wc[1][:, tap, row], hi)]
                if t != 0:
                    for tap in range(HT):
                        hi, lo = (hs[j][:, bs, tap:tap + W] for j in range(2))
                        parts += [(wc[0][:, XT + tap, row], hi), (wc[0][:, XT + tap, row], lo),
                                  (wc[1][:, XT + tap, row], hi)]
                out = gate_ps[k][:, :].rearrange("c (b w) -> c b w", b=GB)
                for n, (w, v) in enumerate(parts):
                    if k == 0 and n == 3 * XT:
                        pe.wait_ge(hlo_done, r.count(2, g - 1))
                    last = nc.tensor.matmul(out, w, v, start=(n == 0), stop=(n == len(parts) - 1))
                last.then_inc(gate_done, 1)

            def row(r, ln1, fin1, gates, ln2, ffn, t):
                if gates:
                    pe.wait_ge(nlo_done[1], r.count(1, 1))
                    gate(r, 0, 0, t)
                if ln1:
                    pe.wait_ge(lo_done[1], r.count(1, 3))
                    if t is None or t >= 2:
                        pe.wait_ge(u_done[2], r.count(1, -1))
                    elif t >= -1:
                        pe.wait_ge(d_done[1], r.count(1, 2))
                    sums(p_ps, 1, mean_done)
                if ffn:
                    pe.wait_ge(nlo_done[2], r.count(1, -1))
                    if not ln1 and t > 2:
                        pe.wait_ge(ev_done, t - 2)
                    pe.wait_ge(u_done[1], r.count(1, 2) if t is None or t + 2 <= H else H)
                    for b in range(2):
                        c = slice(b * N, (b + 1) * N)
                        last = passes(q_ps[:, c], [(wf[0], yn[0][:, c]), (wf[0], yn[1][:, c]), (wf[1], yn[0][:, c])])
                    last.then_inc(ffn_done, 1)
                if gates:
                    gate(r, 0, 1, t)
                if ln2:
                    pe.wait_ge(lo_done[2], r.count(1))
                    if t is None or t + 2 < H:
                        pe.wait_ge(d_done[1], r.count(1, 3))
                    if t is not None and t + 2 >= H and t >= 2:
                        pe.wait_ge(u_done[2], t - 1)
                    sums(p_ps, 2, mean_done)
                if gates:
                    gate(r, 0, 2, t)
                    gate(r, 0, 3, t)
                if ln1:
                    pe.wait_ge(sqlo_done[1], r.count(1, 3))
                    if ffn:
                        pe.wait_ge(ev_done, r.count(1, -1))
                    elif t >= -1:
                        pe.wait_ge(u_done[1], r.count(1, 2))
                    sums(q_ps, 1, var_done)
                if gates:
                    gate(r, 1, 0, t)
                if ln2:
                    pe.wait_ge(sqlo_done[2], r.count(1))
                    sums(p_ps, 2, var_done)
                if gates:
                    for k in range(1, 4):
                        gate(r, 1, k, t)

            rows(pe, row)

            def vy(q, y, n):
                nc.tensor.matmul(gate_ps[q][:, 0:y.shape[1]], v_sb, y, start=True, stop=True).then_inc(vy_done[q], 1)

            for j in range(1, WARM):
                for q in range(Q):
                    pe.wait_ge(y_done[q], j)
                    vy(q, warm_columns(warm_y[(j - 1) % 2], q), j)
            for q in range(Q):
                pe.wait_ge(y_done[q], WARM)
                vy(q, warm_y[(WARM - 1) % 2][:, q * QC:(q + 1) * QC], WARM)
            for w in range(1, SW):
                for q in range(Q):
                    pe.wait_ge(y_done[q], WARM + w)
                    vy(q, columns(slot_of(0) * SLOT, q, w - 1), WARM + w)
            with pe.Fori(1, SLICES) as ws:
                here = pe.snap(slot_of(ws) * SLOT)
                before = pe.snap(slot_of(ws + -1) * SLOT)
                for w in range(SW):
                    for q in range(Q):
                        pe.wait_ge(y_done[q], ws * SW + (WARM + w))
                        vy(q, columns(here, q, w - 1) if w else columns(before, q, SW - 1), None)
            pe.wait_ge(cmp_step, 3)
            nc.tensor.matmul(p_ps[:, 0:1], ones_f, same, start=True, stop=True).then_inc(cmp_sum, 1)
            pe.wait_ge(flag_ready, 1)
            f = pe.value_load(flag[0:1, 0:1])
            with pe.If(f < 1):
                with pe.Fori(0, H * SLICES) as n:
                    for w in range(SW):
                        pe.wait_ge(ex_y, n * SW + (w + 1))
                        nc.tensor.matmul(p_ps[:, 0:B], v_sb, ex_state, start=True, stop=True).then_inc(ex_vy, 1)
            pe.nop()

        @block.scalar
        def _(act):
            act.wait_ge(ready0, 1)

            def squares(r, ln):
                act.wait_ge(d_done[ln], r.count(1, 1))
                nc.scalar.activation(sq[ln], d[ln], ACT.Square)
                nc.scalar.activation(split[ln][0], d[ln], ACT.Square).then_inc(sqhi_done[ln], 1)

            def row(r, ln1, fin1, gates, ln2, ffn, t):
                ahead, after, before, done = r + 2, r + 1, r + -1, r + -2
                if ln1:
                    act.wait_ge(x_in[ahead.p], ahead.pair(16, 16))
                    if t is None or t >= -1:
                        act.wait_ge(var_done[1], ahead.count(1))
                    nc.scalar.copy(split[1][0], x_ring[:, bass.ds(slot4(ahead), 1), :].rearrange("c r n -> c (r n)")
                                   ).then_inc(hi_done[1], 1)
                if fin1:
                    act.wait_ge(norm_done[1], after.count(1, 1))
                    if gates and (t is None or t >= 1):
                        act.wait_ge(gate_done, r.count(8))
                    nc.scalar.copy(xn[after.p][0][:, :, 1:W + 1], d[1].rearrange("c (b w) -> c b w", b=B)
                                   ).then_inc(nhi_done[1], 1)
                if ln2:
                    act.wait_ge(x1_done, before.count(2, 2))
                    if t is None or t >= 2:
                        act.wait_ge(var_done[2], before.count(1))
                    nc.scalar.copy(split[2][0], x1[before.p]).then_inc(hi_done[2], 1)
                if gates:
                    gate_g(r, 0, t)
                if ln1:
                    if t is None or t >= -1:
                        act.wait_ge(w_done[1], ahead.count(1))
                    squares(ahead, 1)
                if gates:
                    gate_i(r, 0)
                if ffn:
                    act.wait_ge(ffn_done, done.count(1, 1))
                    if t is None or t >= 4:
                        act.wait_ge(wx_out[done.p], done.pair(48))
                        act.wait_ge(bn_done, done.count(1, -1))
                    nc.scalar.activation(stage[done.p], q_ps[:, :], ACT.Copy, scale=unscale[:, 4:5]).then_inc(ev_done, 1)
                if ln2:
                    if t is None or t >= 2:
                        act.wait_ge(w_done[2], before.count(1))
                    squares(before, 2)
                if gates:
                    gate_f(r, 0)
                    gate_c(r, 0)
                    gate_o(r, 0)
                    gate_h(r, 0, t)
                    gate_g(r, 1, t)
                lns = ([(2, before)] if ln2 else []) + ([(1, ahead)] if ln1 else [])
                if lns:
                    nc.scalar.preload_act_table_set("natural_log_exp_and_others")
                for ln, rr in lns:
                    act.wait_ge(var_done[ln], rr.count(1, 1))
                    if ln == 1:
                        if t is None or t >= -1:
                            act.wait_ge(norm_done[1], rr.count(1))
                    elif t is None or t >= 2:
                        act.wait_ge(norm_done[2], rr.count(1))
                    nc.scalar.activation(rs[ln], var_ps[ln][:, :], ACT.Ln, bias=eps[ln]).then_inc(ln_done[ln], 1)
                for ln, rr in lns:
                    act.wait_ge(ln_done[ln], rr.count(1, 1))
                    nc.scalar.activation(rs[ln], rs[ln], ACT.Exp, scale=-0.5).then_inc(exp_done[ln], 1)
                for ln, rr in lns:
                    act.wait_ge(exp_done[ln], rr.count(1, 1))
                    nc.scalar.activation(sq[ln], rs[ln], ACT.Square).then_inc(rsq_done[ln], 1)
                if gates:
                    gate_i(r, 1)
                if ln2:
                    act.wait_ge(norm_done[2], before.count(1, 1))
                    if t is None or t >= 2:
                        act.wait_ge(ffn_done, before.count(1))
                    nc.scalar.copy(yn[0], d[2]).then_inc(nhi_done[2], 1)
                if gates:
                    gate_f(r, 1)
                    gate_c(r, 1)
                    gate_o(r, 1)
                    gate_h(r, 1, t)

            def gate_g(r, g, t):
                act.wait_ge(gate_done, r.count(8, 4 * g + 1))
                if t != 0 or g:
                    act.wait_ge(c_done, r.count(2, g))
                nc.scalar.activation(gg, gate_ps[0][:, :], ACT.Tanh, bias=bias[:, 3:4], scale=unscale[:, 3:4]).then_inc(g_done, 1)

            def sigmoid(r, g, k, done):
                act.wait_ge(gate_done, r.count(8, 4 * g + k + 1))
                b = GATE_ROWS[k]
                nc.scalar.activation(gate_ps[k][:, :], gate_ps[k][:, :], ACT.Sigmoid, bias=bias[:, b:b + 1],
                                     scale=unscale[:, b:b + 1]).then_inc(done, 1)

            def gate_i(r, g):
                sigmoid(r, g, 1, i_done)

            def gate_f(r, g):
                sigmoid(r, g, 2, f_done)

            def gate_c(r, g):
                act.wait_ge(c_done, r.count(2, g + 1))
                nc.scalar.activation(hh[g], cell[g], ACT.Tanh).then_inc(tc_done, 1)

            def gate_o(r, g):
                sigmoid(r, g, 3, o_done)

            def gate_h(r, g, t):
                act.wait_ge(h_done, r.count(2, g + 1))
                nc.scalar.activation(hs[0][:, g * GB:(g + 1) * GB, 1:W + 1], hh[g].rearrange("c (b w) -> c b w", b=GB),
                                     ACT.Copy, scale=OPERAND_SCALE).then_inc(hhi_done, 1)

            rows(act, row)

            act.wait_ge(bn_ready, 1)
            for q in range(Q):
                if q == 0:
                    for p in range(2):
                        act.wait_ge(wx_out[p], 48 * H // 2)
                nc.scalar.activation(warm_columns(warm_y[0], q), warm_source(0, q), ACT.Sigmoid, bias=bn_b,
                                     scale=bn_s).then_inc(y_done[q], 1)
            for j in range(1, WARM):
                for q in range(Q):
                    act.wait_ge(z_done[q], j)
                    y = warm_columns(warm_y[j % 2], q)
                    nc.scalar.activation(y, gate_ps[q][:, 0:y.shape[1]], ACT.Sigmoid, bias=bn_b).then_inc(y_done[q], 1)
            with act.Fori(0, SLICES) as ws:
                here = act.snap(slot_of(ws) * SLOT)
                for w in range(SW):
                    for q in range(Q):
                        act.wait_ge(z_done[q], ws * SW + (WARM + w))
                        nc.scalar.activation(columns(here, q, w), gate_ps[q][:, 0:QC], ACT.Sigmoid,
                                             bias=bn_b).then_inc(y_done[q], 1)
            act.wait_ge(flag_ready, 1)
            f = act.value_load(flag[0:1, 0:1])
            with act.If(f < 1):
                with act.Fori(0, H * SLICES) as n:
                    for w in range(SW):
                        act.wait_ge(ex_z, n * SW + (w + 1))
                        act.wait_ge(ex_add, n * SW + w)
                        nc.scalar.activation(ex_state, p_ps[:, 0:B], ACT.Sigmoid, bias=bn_b).then_inc(ex_y, 1)
            act.nop()

        @block.gpsimd
        def _(pool):
            pool.wait_ge(prep, 2)
            nc.gpsimd.partition_all_reduce(most_all, most, C, bass.bass_isa.ReduceOp.max).then_inc(prep_pool, 1)
            nc.gpsimd.partition_all_reduce(least_all, least, C, bass.bass_isa.ReduceOp.max).then_inc(prep_pool, 1)
            pool.wait_ge(ready0, 1)

            def squares_lo(r, ln):
                pool.wait_ge(sqhi_done[ln], r.count(1, 1))
                nc.gpsimd.tensor_tensor(split[ln][1], sq[ln], split[ln][0], ALU.subtract).then_inc(sqlo_done[ln], 1)

            def row(r, ln1, fin1, gates, ln2, ffn, t):
                after = r + 1
                if fin1:
                    pool.wait_ge(nhi_done[1], after.count(1, 1))
                    nc.gpsimd.tensor_tensor(xn[after.p][1][:, :, 1:W + 1], d[1].rearrange("c (b w) -> c b w", b=B),
                                            xn[after.p][0][:, :, 1:W + 1], ALU.subtract).then_inc(nlo_done[1], 1)
                if ln1:
                    squares_lo(r + 2, 1)
                if ln2:
                    squares_lo(r + -1, 2)
                    pool.wait_ge(nhi_done[2], (r + -1).count(1, 1))
                    nc.gpsimd.tensor_tensor(yn[1], d[2], yn[0], ALU.subtract).then_inc(nlo_done[2], 1)

            rows(pool, row)

            pool.wait_ge(bn_step, 2)
            nc.gpsimd.tensor_tensor(bn_s, bn_t, half, ALU.pow).then_inc(bn_step, 1)

            for p in range(2):
                pool.wait_ge(x1_out[p], 32 * H // 2)
            for ws in range(SLICES):
                for q in range(Q):
                    pool.wait_ge(y_done[q], WARM + (ws + 1) * SW)
                s = slot_of(ws)
                pool.dma_start(out_d[:, ws, :, :].rearrange("c h n -> c (h n)"), slices[:, s * SLOT:(s + 1) * SLOT],
                               accum_op=ALU.add, max_dma_last_dim=2048).then_inc(slice_out[ws], 16)
            for ws in range(SLICES):
                pool.wait_ge(slice_out[ws], 16)

        @block.vector
        def _(dve):
            def step(ins, sem_, count):
                ins.then_inc(sem_, 1)
                dve.wait_ge(sem_, count)

            dve.wait_ge(loaded, 16 * LOADS)
            by_gate = raw_c.rearrange("c k g o -> c g k o")
            nc.vector.tensor_reduce(most[:, 0:4], by_gate, AX.XY, ALU.max)
            nc.vector.tensor_reduce(least[:, 0:4], by_gate, AX.XY, ALU.min, negate=True)
            nc.vector.tensor_reduce(most[:, 4:5], raw_f, AX.X, ALU.max).then_inc(prep, 1)
            nc.vector.tensor_reduce(least[:, 4:5], raw_f, AX.X, ALU.min, negate=True).then_inc(prep, 1)
            nc.vector.tensor_tensor(bias, bias_is, bias_ss, ALU.add)
            nc.vector.memset(eps[1], CONV_EPS)
            nc.vector.memset(eps[2], TOKEN_EPS)
            nc.vector.memset(half, -0.5)
            nc.vector.memset(ones_bf, 1.0 / C)
            for r in range(2):
                for j in range(2):
                    nc.vector.memset(xn[r][j][:, :, 0:1], 0.0)
            for j in range(2):
                nc.vector.memset(hs[j][:, :, 0:1], 0.0)
                nc.vector.memset(hs[j][:, :, W + 1:W + 2], 0.0)
            for g in range(G):
                nc.vector.memset(cell[g], 0.0)
            dve.wait_ge(prep_pool, 2)
            step(nc.vector.tensor_tensor(most_all, most_all, least_all, ALU.max), prep, 3)
            step(nc.vector.tensor_scalar(most_all, most_all, 2.0 ** -60, None, ALU.max), prep, 4)
            step(nc.vector.tensor_scalar(most_all.bitcast(I32), most_all.bitcast(I32), 0x7F800000, None,
                                         ALU.bitwise_and), prep, 5)
            step(nc.vector.reciprocal(rescale, most_all), prep, 6)
            step(nc.vector.tensor_scalar(rescale, rescale, WEIGHT_SCALE, None, ALU.mult), prep, 7)
            nc.vector.tensor_scalar(unscale, most_all, 1.0 / (WEIGHT_SCALE * OPERAND_SCALE), None, ALU.mult)
            for g in range(4):
                nc.vector.tensor_scalar(wc[0][:, :, g], raw_c[:, :, g], rescale[:, g:g + 1], None, ALU.mult)
            step(nc.vector.tensor_scalar(wf[0], raw_f, rescale[:, 4:5], None, ALU.mult), prep, 8)
            for g in range(4):
                nc.vector.scalar_tensor_tensor(wc[1][:, :, g], raw_c[:, :, g], rescale[:, g:g + 1], wc[0][:, :, g],
                                               ALU.mult, ALU.subtract)
            nc.vector.scalar_tensor_tensor(wf[1], raw_f, rescale[:, 4:5], wf[0], ALU.mult,
                                           ALU.subtract).then_inc(ready0, 1)

            def lo_part(r, ln, src):
                dve.wait_ge(hi_done[ln], r.count(1, 1))
                nc.vector.tensor_tensor(split[ln][1], src, split[ln][0], ALU.subtract).then_inc(lo_done[ln], 1)

            def centre(r, ln, src):
                dve.wait_ge(mean_done[ln], r.count(1, 1))
                nc.vector.tensor_tensor(d[ln], src, mean_ps[ln][:, :], ALU.subtract).then_inc(d_done[ln], 1)

            def norm(r, ln):
                dve.wait_ge(rsq_done[ln], r.count(1, 1))
                step(nc.vector.scalar_tensor_tensor(sq[ln], var_ps[ln][:, :], (0, CONV_EPS, TOKEN_EPS)[ln], sq[ln],
                                                    ALU.add, ALU.mult), u_done[ln], r.count(1, 1))
                step(nc.vector.scalar_tensor_tensor(rs[ln], sq[ln], 3.0, rs[ln], ALU.subtract, ALU.mult),
                     w_done[ln], r.count(1, 1))
                nc.vector.scalar_tensor_tensor(d[ln], rs[ln], -0.5 * OPERAND_SCALE, d[ln], ALU.mult,
                                               ALU.mult).then_inc(norm_done[ln], 1)

            def x_of(r):
                return x_ring[:, bass.ds(slot4(r), 1), :].rearrange("c r n -> c (r n)")

            def gate_i(r, g):
                dve.wait_ge(i_done, r.count(2, g + 1))
                nc.vector.tensor_tensor(gg, gate_ps[1][:, :], gg, ALU.mult).then_inc(ig_done, 1)

            def gate_f(r, g):
                dve.wait_ge(f_done, r.count(2, g + 1))
                dve.wait_ge(ig_done, r.count(2, g + 1))
                step(nc.vector.tensor_tensor(cell[g], gate_ps[2][:, :], cell[g], ALU.mult), fc_done, r.count(2, g + 1))
                nc.vector.tensor_tensor(cell[g], cell[g], gg, ALU.add).then_inc(c_done, 1)

            def gate_o(r, g, t):
                dve.wait_ge(o_done, r.count(2, g + 1))
                step(nc.vector.tensor_tensor(hh[g], gate_ps[3][:, :], hh[g], ALU.mult), h_done, r.count(2, g + 1))
                if t is None or t >= 2:
                    dve.wait_ge(x1_out[r.p], r.pair(32))
                dst = x1[r.p].rearrange("c (s b w) -> c s b w", s=SLICES, b=B)[:, :, g * GB:(g + 1) * GB, :]
                src = x_ring[:, bass.ds(slot4(r), 1), g * N:(g + 1) * N].rearrange("c r (b s w) -> c s (r b) w", b=GB, s=SLICES)
                nc.vector.tensor_tensor(dst, hh[g].rearrange("c (b s w) -> c s b w", b=GB, s=SLICES), src,
                                        ALU.add).then_inc(x1_done, 1)
                dve.wait_ge(hhi_done, r.count(2, g + 1))
                own = slice(g * GB, (g + 1) * GB)
                nc.vector.scalar_tensor_tensor(hs[1][:, own, 1:W + 1], hh[g].rearrange("c (b w) -> c b w", b=GB),
                                               OPERAND_SCALE, hs[0][:, own, 1:W + 1], ALU.mult,
                                               ALU.subtract).then_inc(hlo_done, 1)

            def row(r, ln1, fin1, gates, ln2, ffn, t):
                ahead, before, done = r + 2, r + -1, r + -2
                if ln1:
                    lo_part(ahead, 1, x_of(ahead))
                if ln2:
                    lo_part(before, 2, x1[before.p])
                if ln1:
                    if fin1:
                        dve.wait_ge(nlo_done[1], ahead.count(1))
                    centre(ahead, 1, x_of(ahead))
                if gates:
                    gate_i(r, 0)
                if ln2:
                    if t is None or t >= 2:
                        dve.wait_ge(nlo_done[2], before.count(1))
                    centre(before, 2, x1[before.p])
                if gates:
                    gate_f(r, 0)
                if ffn:
                    dve.wait_ge(ev_done, done.count(1, 1))
                    for b in range(2):
                        ins = nc.vector.bn_stats(bn_parts[:, bass.ds(done.count(2, b), 1), :],
                                                 stage[done.p][:, b * N:(b + 1) * N])
                    ins.then_inc(bn_done, 1)
                if gates:
                    gate_o(r, 0, t)
                if ln2:
                    norm(before, 2)
                if gates:
                    gate_i(r, 1)
                if ln1:
                    norm(ahead, 1)
                if gates:
                    gate_f(r, 1)
                    gate_o(r, 1, t)

            rows(dve, row)

            dve.wait_ge(bn_done, H)
            step(nc.vector.bn_aggr(bn, bn_parts.rearrange("c r s -> c (r s)")), bn_step, 1)
            nc.vector.tensor_scalar(bn_t, bn[:, 1:2], BN_EPS, None, ALU.add).then_inc(bn_step, 1)
            dve.wait_ge(bn_step, 3)
            step(nc.vector.tensor_tensor(bn_s, bn_s, gamma, ALU.mult), bn_step, 4)
            step(nc.vector.tensor_tensor(bn_t, bn[:, 0:1], bn_s, ALU.mult), bn_step, 5)
            nc.vector.tensor_tensor(bn_b, beta, bn_t, ALU.subtract)
            for j in range(2):
                nc.vector.memset(warm_y[j][:, 0:B], 0.0)
            nc.vector.memset(ones_f, 1.0).then_inc(bn_ready, 1)

            def z(q, wx):
                out = gate_ps[q][:, 0:wx.shape[1]]
                nc.vector.scalar_tensor_tensor(out, wx, bn_s, out, ALU.mult, ALU.add).then_inc(z_done[q], 1)

            for j in range(1, WARM):
                for q in range(Q):
                    dve.wait_ge(vy_done[q], j)
                    z(q, warm_source(j, q))
            for first, last in ((0, FIRST_KEPT), (FIRST_KEPT, SLICES)):
                with dve.Fori(first, last) as ws:
                    here = dve.snap(slot_of(ws) * SLOT)
                    if last == FIRST_KEPT:
                        dve.wait_ge(slice_in, ws * 16 + 16)
                    for w in range(SW):
                        for q in range(Q):
                            dve.wait_ge(vy_done[q], ws * SW + (WARM + w))
                            z(q, columns(here, q, w))

            for q in range(Q):
                dve.wait_ge(y_done[q], WARM + W)
            ended = slices[:, bass.ds(slot_of(SLICES - 1) * SLOT + SW - 1, COMPARED, step=SW)]
            gap = warm_y[WARM % 2][:, 0:COMPARED]
            step(nc.vector.tensor_tensor(gap, warm_y[(WARM - 1) % 2][:, B:ROW], ended, ALU.subtract), cmp_step, 1)
            step(nc.vector.tensor_tensor(gap, gap, gap, ALU.mult), cmp_step, 2)
            nc.vector.tensor_scalar(gap, gap, TOLERANCE ** 2, None, ALU.is_le, ALU.add, accum_out=same).then_inc(cmp_step, 1)
            dve.wait_ge(cmp_sum, 1)
            want = float(COMPARED * C) if not force_exact else -1.0
            nc.vector.tensor_scalar(flag, p_ps[:, 0:1], want, None, ALU.is_equal).then_inc(flag_ready, 1)
            dve.wait_ge(flag_ready, 1)
            f = dve.value_load(flag[0:1, 0:1])
            with dve.If(f < 1):
                nc.vector.memset(ex_state, 0.0).then_inc(ex_y, 1)
                with dve.Fori(0, H * SLICES) as n:
                    ws = dve.snap(n % SLICES)
                    dve.wait_ge(ex_in, n // SLICES * 32 + 32)
                    for w in range(SW):
                        dve.wait_ge(ex_vy, n * SW + (w + 1))
                        own = bass.ds(ws * SC + w, B, step=SW)
                        nc.vector.scalar_tensor_tensor(p_ps[:, 0:B], slices[:, own], bn_s, p_ps[:, 0:B], ALU.mult,
                                                       ALU.add).then_inc(ex_z, 1)
                        dve.wait_ge(ex_y, n * SW + (w + 2))
                        add = slices[:, bass.ds(ws * SC + (ROW + w), B, step=SW)]
                        nc.vector.tensor_tensor(add, add, ex_state, ALU.add).then_inc(ex_add, 1)
            dve.nop()


_OUT = (C, SLICES, H, B, SW)


def kernel(x, L0_conv_W_is, L0_conv_b_is, L0_conv_W_ss, L0_conv_b_ss, L0_ffn_W, L0_ffn_V, L0_ffn_gamma, L0_ffn_beta):
    import numpy as np
    import concourse.bacc as bacc
    from concourse.bass_utils import run_bass_kernel_spmd

    def taps(w, n):
        return np.asarray(w)[:, :, 0, :n].reshape(4, C, C, n).transpose(2, 3, 0, 1)

    arrays = {
        "x": np.asarray(x).transpose(1, 2, 0, 3).reshape(C, H, ROW),
        "w_is": taps(L0_conv_W_is, XT), "w_ss": taps(L0_conv_W_ss, HT),
        "b_is": np.asarray(L0_conv_b_is).reshape(4, C).T, "b_ss": np.asarray(L0_conv_b_ss).reshape(4, C).T,
        "ffn_w": np.asarray(L0_ffn_W).T, "ffn_v": np.asarray(L0_ffn_V).T,
        "gamma": np.asarray(L0_ffn_gamma).reshape(C, 1), "beta": np.asarray(L0_ffn_beta).reshape(C, 1),
    }
    arrays = {k: np.ascontiguousarray(v) for k, v in arrays.items()}
    nc = bacc.Bacc("TRN2", target_bir_lowering=False, num_devices=1)
    args = [nc.dram_tensor(k, v.shape, mybir.dt.from_np(v.dtype), kind="ExternalInput").ap() for k, v in arrays.items()]
    out = nc.dram_tensor("out", (C, SLICES, H, SC), F32, kind="ExternalOutput").ap()
    build(nc, *args, out)
    r = run_bass_kernel_spmd(nc, [arrays], core_ids=[0])
    return r.results[0]["out"].reshape(_OUT).transpose(3, 0, 2, 1, 4).reshape(B, C, H, W)
```

```python
from contextlib import ExitStack

import concourse.bass as bass
from concourse import mybir

F32, F16, BF16 = mybir.dt.float32, mybir.dt.float16, mybir.dt.bfloat16
I32 = mybir.dt.int32
ALU = mybir.AluOpType
ACT = mybir.ActivationFunctionType
AX = mybir.AxisListType

B, C, H, W = 16, 128, 64, 64
G = 2
GB = B // G
N = GB * W
ROW = B * W
GATE_ROWS = (3, 0, 1, 2)
XT, HT = 2, 3
TAPS = XT + HT
SW = 8
SLICES = W // SW
SC = B * SW
RING, FIRST_KEPT = 3, 5
SLOT = H * SC
Q = 5
Q_FIRST = [-(-H * q // Q) for q in range(Q + 1)]
WARM = 12
CONV_EPS, TOKEN_EPS, BN_EPS = 1e-6, 1e-5, 1e-5
OPERAND_SCALE = 2.0 ** 11
WEIGHT_SCALE = 2.0 ** 14
TOLERANCE = 2.0 ** -22
COMPARED = (H - 1) * B


def slot_of(ws):
    return ws % RING + RING * (ws // FIRST_KEPT)


class Row:

    def __init__(self, i, off):
        self.i, self.off, self.p = i, off, off % 2

    def __add__(self, d):
        return Row(self.i, self.off + d)

    def count(self, per_row, more=0):
        return self.i * (2 * per_row) + (per_row * self.off + more)

    def pair(self, each, more=0):
        return self.i * each + (each * (self.off // 2) + more)


def build(nc, x_d, wis_d, wss_d, bis_d, bss_d, wf_d, v_d, gamma_d, beta_d, out_d, force_exact=False):
    x1_d = nc.dram_tensor("x1_scratch", (C, SLICES, H, SC), F32, kind="Internal").ap()
    wx_d = nc.dram_tensor("wx_scratch", (C, SLICES, H, SC), F32, kind="Internal").ap()
    ctx = ExitStack()
    with ctx:
        def sem(name):
            return ctx.enter_context(nc.semaphore(name))

        slices = ctx.enter_context(nc.sbuf_tensor("slices", [C, 2 * RING * SLOT], F32))
        extra = ctx.enter_context(nc.sbuf_tensor("extra", [C, 3968], F32))
        taken = {"slices": 0, "extra": 0}

        def carve(size, dt=F32, of="slices"):
            words = size if dt in (F32, I32) else (size + 1) // 2
            words += words % 2
            a = taken[of]
            taken[of] = a + words
            assert taken[of] <= (RING * SLOT if of == "slices" else 3968), (of, taken)
            v = (slices if of == "slices" else extra)[:, a:a + words]
            return v if dt == F32 else v.bitcast(dt)[:, 0:size]

        x_ring = carve(4 * ROW).rearrange("c (r n) -> c r n", r=4)
        x1 = [carve(ROW) for _ in range(2)]
        split = {ln: (carve(ROW, BF16), carve(ROW, BF16)) for ln in (1, 2)}
        d = {ln: carve(ROW) for ln in (1, 2)}
        sq = {ln: carve(ROW) for ln in (1, 2)}
        rs = {ln: carve(ROW) for ln in (1, 2)}
        xn = [[carve(B * (W + 1), F16).rearrange("c (b w) -> c b w", b=B) for _ in range(2)] for _ in range(2)]
        yn = [carve(ROW, F16) for _ in range(2)]
        hs = [carve(B * (W + 2), F16).rearrange("c (b w) -> c b w", b=B) for _ in range(2)]
        stage = [carve(ROW) for _ in range(2)]
        assert SLOT <= 4 * ROW + 2 * ROW + 2 * ROW
        wc = [carve(TAPS * 4 * C, F16).rearrange("c (k g o) -> c k g o", k=TAPS, g=4) for _ in range(2)]
        wf = [carve(C, F16, "extra") for _ in range(2)]
        ones_bf = carve(C, BF16, "extra")
        bn_parts = carve(H * 2 * 6, F32, "extra").rearrange("c (r s) -> c r s", s=6)
        v_sb = carve(C, F32, "extra")
        small = carve(64, F32, "extra")
        raw = slices[:, RING * SLOT:RING * SLOT + (TAPS * 4 + 1) * C]
        raw_c = raw[:, 0:TAPS * 4 * C].rearrange("c (k g o) -> c k g o", k=TAPS, g=4)
        raw_f = raw[:, TAPS * 4 * C:]
        ones_f = carve(C, F32, "extra")
        cells = carve(5 * N, F32, "extra")
        cell = [cells[:, g * N:(g + 1) * N] for g in range(G)]
        gg = cells[:, 2 * N:3 * N]
        hh = [cells[:, (3 + g) * N:(4 + g) * N] for g in range(G)]
        warm_y = [cells[:, j * ROW:(j + 1) * ROW] for j in range(2)]

        bias_is, bias_ss, bias = small[:, 0:4], small[:, 4:8], small[:, 8:12]
        gamma, beta = small[:, 12:13], small[:, 13:14]
        most, least = small[:, 14:19], small[:, 20:25]
        most_all, least_all = small[:, 26:31], small[:, 32:37]
        unscale, rescale = small[:, 38:43], small[:, 44:49]
        eps = {1: small[:, 50:51], 2: small[:, 51:52]}
        bn, bn_s, bn_b, half = small[:, 52:54], small[:, 54:55], small[:, 55:56], small[:, 56:57]
        same, flag = small[:, 57:58], small[:, 58:59].bitcast(I32)
        bn_t = small[:, 59:60]

        gate_ps = [ctx.enter_context(nc.psum_tensor(f"gate_ps{k}", [C, N], F32)) for k in range(4)]
        p_ps = ctx.enter_context(nc.psum_tensor("p_ps", [C, ROW], F32))
        q_ps = ctx.enter_context(nc.psum_tensor("q_ps", [C, ROW], F32))
        mean_ps, var_ps = {1: p_ps, 2: p_ps}, {1: q_ps, 2: p_ps}
        z_ps = [*gate_ps, p_ps[:, 0:N]]

        loaded, constants, weights_ready = sem("loaded"), sem("constants"), sem("weights_ready")
        prep, prep_pool = sem("prep"), sem("prep_pool")
        x_in = [sem(f"x_in{p}") for p in range(2)]
        x1_out = [sem(f"x1_out{p}") for p in range(2)]
        wx_out = [sem(f"wx_out{p}") for p in range(2)]
        hi_done, lo_done, mean_done, d_done, sqhi_done, sqlo_done, var_done, ln_done, exp_done, rsq_done, u_done, w_done, \
            norm_done, nhi_done, nlo_done = (
                {ln: sem(f"{name}{ln}") for ln in (1, 2)} for name in (
                    "hi", "lo", "mean", "d", "sqhi", "sqlo", "var", "ln", "exp", "rsq", "u", "w", "norm", "nhi", "nlo"))
        gate_done, g_done, i_done, f_done, o_done, tc_done = (sem(s) for s in ("gate", "g", "i", "f", "o", "tc"))
        ig_done, fc_done, c_done, h_done, hhi_done, hlo_done, x1_done = (
            sem(s) for s in ("ig", "fc", "c", "h", "hhi", "hlo", "x1"))
        ffn_done, ev_done, bn_done = sem("ffn"), sem("ev"), sem("bn_part")
        bn_step, bn_ready = sem("bn_step"), sem("bn_ready")
        early_in, slice_in = sem("early_in"), sem("slice_in")
        slice_out = [sem(f"slice_out{ws}") for ws in range(SLICES)]
        vy_done, z_done, y_done = ([sem(f"{s}{q}") for q in range(Q)] for s in ("vy", "z", "y"))
        cmp_step, cmp_sum, flag_ready = sem("cmp_step"), sem("cmp_sum"), sem("flag_ready")
        ex_in, ex_out, ex_vy, ex_z, ex_y, ex_add = (sem(s) for s in ("ex_in", "ex_out", "ex_vy", "ex_z", "ex_y", "ex_add"))

        ex_wx = slices[:, 0:ROW].rearrange("c (s n) -> c s n", s=SLICES)
        ex_x1 = slices[:, ROW:2 * ROW].rearrange("c (s n) -> c s n", s=SLICES)
        ex_state = cells[:, 4 * N:4 * N + B]

        block = ctx.enter_context(nc.Block())

        LOADS = 8

        def rows(engine, row):
            def one(t):
                row(Row(t // 2, t % 2), split1=t + 3 < H, ln1=t + 2 < H, gates=0 <= t < H, ln2=0 <= t - 1 < H,
                    ffn=0 <= t - 2 < H, t=t)
            for t in range(-2, 4):
                one(t)
            with engine.Fori(2, (H - 4) // 2) as i:
                for p in range(2):
                    row(Row(i, p), split1=True, ln1=True, gates=True, ln2=True, ffn=True, t=None)
            for t in range(H - 4, H + 2):
                one(t)

        def dve_splits(t):
            return t is not None and (t < 0 or t == H)

        def squares_lo(engine, eng, r, ln):
            engine.wait_ge(sqhi_done[ln], r.count(1, 1))
            eng.tensor_tensor(split[ln][1], sq[ln], split[ln][0], ALU.subtract).then_inc(sqlo_done[ln], 1)

        def normed_x_lo(engine, eng, r):
            engine.wait_ge(nhi_done[1], r.count(1, 1))
            eng.tensor_tensor(xn[r.p][1][:, :, 1:W + 1], d[1].rearrange("c (b w) -> c b w", b=B),
                              xn[r.p][0][:, :, 1:W + 1], ALU.subtract).then_inc(nlo_done[1], 1)

        def normed_x1_lo(engine, eng, r):
            engine.wait_ge(nhi_done[2], r.count(1, 1))
            eng.tensor_tensor(yn[1], d[2], yn[0], ALU.subtract).then_inc(nlo_done[2], 1)

        def slot4(row):
            return row.count(1) % 4

        def group(v, g):
            return v[:, g * N:(g + 1) * N].rearrange("c (b w) -> c b w", b=GB)

        def q_columns(q):
            return (Q_FIRST[q + 1] - Q_FIRST[q]) * B

        def columns(at, q, w):
            return slices[:, bass.ds(at + (Q_FIRST[q] * SC + w), q_columns(q), step=SW)]

        def warm_columns(tile, q):
            return tile[:, max(Q_FIRST[q], 1) * B:Q_FIRST[q + 1] * B]

        def warm_source(j, q):
            w = W - WARM + j
            first = max(Q_FIRST[q], 1) - 1
            a = slot_of(w // SW) * SLOT + first * SC + w % SW
            return slices[:, bass.ds(a, (Q_FIRST[q + 1] - 1 - first) * B, step=SW)]

        @block.sync
        def _(sp):
            def load_x(r, t):
                if t is None or t >= 4:
                    sp.wait_ge(x1_done, r.count(2, -6))
                elif t >= 2:
                    sp.wait_ge(x_in[r.p], r.pair(16))
                sp.dma_start(x_ring[:, bass.ds(slot4(r), 1), :], x_d[:, bass.ds(r.count(1), 1), :]).then_inc(x_in[r.p], 16)

            def load_slice(ws, first, last, done):
                a = slot_of(ws) * SLOT
                sp.dma_start(slices[:, a + first * SC:a + last * SC],
                             wx_d[:, ws, first:last, :].rearrange("c h n -> c (h n)")).then_inc(done, 16)

            load_x(Row(0, 0), 0)
            for dst, src in ((raw_c[:, 0:XT], wis_d), (raw_c[:, XT:TAPS], wss_d), (raw_f, wf_d), (v_sb, v_d),
                             (bias_is, bis_d), (bias_ss, bss_d), (gamma, gamma_d), (beta, beta_d)):
                sp.dma_start(dst, src).then_inc(loaded, 16)

            def row(r, split1, ln1, gates, ln2, ffn, t):
                if t is None or t + 3 < H:
                    load_x(r + 3, None if t is None else t + 3)
                if ln2:
                    r1 = r + -1
                    sp.wait_ge(x1_done, r1.count(2, 2))
                    src = x1[r1.p].rearrange("c (s n) -> c s n", s=SLICES)
                    for dst in (out_d, x1_d):
                        sp.dma_start(dst[:, :, bass.ds(r1.count(1), 1), :].rearrange("c s r n -> c s (r n)"),
                                     src).then_inc(x1_out[r1.p], 16)
                if t == H + 1:
                    sp.wait_ge(wx_out[0], 48 * H // 2)
                    sp.wait_ge(wx_out[1], 48 * (H // 2 - 1))
                    for p in range(2):
                        sp.wait_ge(x1_out[p], 32 * H // 2)
                    sp.wait_ge(var_done[2], H)
                    load_slice(0, 0, H - 1, early_in)
                if ffn:
                    r2 = r + -2
                    sp.wait_ge(ev_done, r2.count(1, 1))
                    src = stage[r2.p].rearrange("c (s n) -> c s n", s=SLICES)
                    sp.dma_start(wx_d[:, :, bass.ds(r2.count(1), 1), :].rearrange("c s r n -> c s (r n)"),
                                 src).then_inc(wx_out[r2.p], 16)
                    kept = slices[:, :].rearrange("c (k h n) -> c k h n", k=2 * RING, h=H)
                    for a, b in ((FIRST_KEPT, FIRST_KEPT + 1), (FIRST_KEPT + 1, SLICES)):
                        s = slot_of(a)
                        sp.dma_start(kept[:, s:s + b - a, bass.ds(r2.count(1), 1), :].rearrange("c s r n -> c s (r n)"),
                                     src[:, a:b, :]).then_inc(wx_out[r2.p], 16)

            rows(sp, row)
            sp.wait_ge(wx_out[1], 48 * H // 2)
            sp.wait_ge(bn_done, H)
            sp.wait_ge(early_in, 16)
            for ws in range(FIRST_KEPT):
                if ws:
                    sp.wait_ge(slice_in, 16 * ws)
                if ws >= RING:
                    sp.wait_ge(slice_out[ws - RING], 16)
                    for q in range(Q):
                        sp.wait_ge(vy_done[q], WARM + (ws - RING + 1) * SW)
                load_slice(ws, 0 if ws else H - 1, H, slice_in)
            for ws in range(SLICES):
                sp.wait_ge(slice_out[ws], 16)
            sp.wait_ge(flag_ready, 1)
            f = sp.value_load(flag[0:1, 0:1])
            with sp.If(f < 1):
                with sp.Fori(0, H) as h:
                    sp.wait_ge(ex_out, h * 16)
                    sp.dma_start(ex_wx, wx_d[:, :, bass.ds(h, 1), :].rearrange("c s r n -> c s (r n)")).then_inc(ex_in, 16)
                    sp.dma_start(ex_x1, x1_d[:, :, bass.ds(h, 1), :].rearrange("c s r n -> c s (r n)")).then_inc(ex_in, 16)
                    sp.wait_ge(ex_add, h * W + W)
                    sp.dma_start(out_d[:, :, bass.ds(h, 1), :].rearrange("c s r n -> c s (r n)"), ex_x1).then_inc(ex_out, 16)
                sp.wait_ge(ex_out, 16 * H)
            sp.nop()

        @block.tensor
        def _(pe):
            pe.wait_ge(constants, 1)

            def passes(out, parts):
                last = None
                for n, (w, v) in enumerate(parts):
                    last = nc.tensor.matmul(out, w, v, start=(n == 0), stop=(n == len(parts) - 1))
                return last

            def sums(ps, ln, done):
                hi, lo = split[ln]
                for b in range(2):
                    c = slice(b * N, (b + 1) * N)
                    last = passes(ps[:, c], [(ones_bf, hi[:, c]), (ones_bf, lo[:, c])])
                last.then_inc(done[ln], 1)

            def gate(r, g, k, t):
                if t != 0 or g:
                    pe.wait_ge((g_done, ig_done, fc_done, h_done)[k], r.count(2, g))
                bs = slice(g * GB, (g + 1) * GB)
                row = GATE_ROWS[k]
                parts = []
                for tap in range(XT):
                    hi, lo = (xn[r.p][j][:, bs, tap:tap + W] for j in range(2))
                    parts += [(wc[0][:, tap, row], hi), (wc[0][:, tap, row], lo), (wc[1][:, tap, row], hi)]
                if t != 0:
                    for tap in range(HT):
                        hi, lo = (hs[j][:, bs, tap:tap + W] for j in range(2))
                        parts += [(wc[0][:, XT + tap, row], hi), (wc[0][:, XT + tap, row], lo),
                                  (wc[1][:, XT + tap, row], hi)]
                out = gate_ps[k][:, :].rearrange("c (b w) -> c b w", b=GB)
                for n, (w, v) in enumerate(parts):
                    if k == 0 and n == 3 * XT:
                        pe.wait_ge(hlo_done, r.count(2, g - 1))
                    last = nc.tensor.matmul(out, w, v, start=(n == 0), stop=(n == len(parts) - 1))
                last.then_inc(gate_done, 1)

            def row(r, split1, ln1, gates, ln2, ffn, t):
                if t == 0:
                    pe.wait_ge(weights_ready, 1)
                if gates:
                    pe.wait_ge(nlo_done[1], r.count(1, 1))
                    gate(r, 0, 0, t)
                if ln1:
                    pe.wait_ge(lo_done[1], r.count(1, 3))
                    if t is None or t >= 2:
                        pe.wait_ge(u_done[2], r.count(1, -1))
                    elif t >= -1:
                        pe.wait_ge(d_done[1], r.count(1, 2))
                    sums(p_ps, 1, mean_done)
                if gates:
                    gate(r, 0, 1, t)
                if ffn:
                    pe.wait_ge(nlo_done[2], r.count(1, -1))
                    if not ln1 and t > 2:
                        pe.wait_ge(ev_done, t - 2)
                    pe.wait_ge(u_done[1], r.count(1, 2) if t is None or t + 2 <= H else H)
                    for b in range(2):
                        c = slice(b * N, (b + 1) * N)
                        last = passes(q_ps[:, c], [(wf[0], yn[0][:, c]), (wf[0], yn[1][:, c]), (wf[1], yn[0][:, c])])
                    last.then_inc(ffn_done, 1)
                if ln2:
                    pe.wait_ge(lo_done[2], r.count(1))
                    if t is None or t + 2 < H:
                        pe.wait_ge(d_done[1], r.count(1, 3))
                    if t is not None and t + 2 >= H and t >= 2:
                        pe.wait_ge(u_done[2], t - 1)
                    sums(p_ps, 2, mean_done)
                if gates:
                    gate(r, 0, 2, t)
                if ln1:
                    pe.wait_ge(sqlo_done[1], r.count(1, 3))
                    if ffn:
                        pe.wait_ge(ev_done, r.count(1, -1))
                    elif t >= -1:
                        pe.wait_ge(u_done[1], r.count(1, 2))
                    sums(q_ps, 1, var_done)
                if gates:
                    gate(r, 0, 3, t)
                if ln2:
                    pe.wait_ge(sqlo_done[2], r.count(1))
                    sums(p_ps, 2, var_done)
                if gates:
                    for k in range(4):
                        gate(r, 1, k, t)

            rows(pe, row)

            def vy(q, y, n):
                nc.tensor.matmul(z_ps[q][:, 0:y.shape[1]], v_sb, y, start=True, stop=True).then_inc(vy_done[q], 1)

            for j in range(1, WARM):
                for q in range(Q):
                    pe.wait_ge(y_done[q], j)
                    vy(q, warm_columns(warm_y[(j - 1) % 2], q), j)
            for q in range(Q):
                pe.wait_ge(y_done[q], WARM)
                vy(q, warm_y[(WARM - 1) % 2][:, Q_FIRST[q] * B:Q_FIRST[q + 1] * B], WARM)
            for w in range(1, SW):
                for q in range(Q):
                    pe.wait_ge(y_done[q], WARM + w)
                    vy(q, columns(slot_of(0) * SLOT, q, w - 1), WARM + w)
            with pe.Fori(1, SLICES) as ws:
                here = pe.snap(slot_of(ws) * SLOT)
                before = pe.snap(slot_of(ws + -1) * SLOT)
                for w in range(SW):
                    for q in range(Q):
                        pe.wait_ge(y_done[q], ws * SW + (WARM + w))
                        vy(q, columns(here, q, w - 1) if w else columns(before, q, SW - 1), None)
            pe.wait_ge(cmp_step, 3)
            nc.tensor.matmul(p_ps[:, 0:1], ones_f, same, start=True, stop=True).then_inc(cmp_sum, 1)
            pe.wait_ge(flag_ready, 1)
            f = pe.value_load(flag[0:1, 0:1])
            with pe.If(f < 1):
                with pe.Fori(0, H * SLICES) as n:
                    for w in range(SW):
                        pe.wait_ge(ex_y, n * SW + (w + 1))
                        nc.tensor.matmul(p_ps[:, 0:B], v_sb, ex_state, start=True, stop=True).then_inc(ex_vy, 1)
            pe.nop()

        @block.scalar
        def _(act):
            act.wait_ge(constants, 1)

            def squares(r, ln):
                act.wait_ge(d_done[ln], r.count(1, 1))
                nc.scalar.activation(sq[ln], d[ln], ACT.Square)
                nc.scalar.activation(split[ln][0], d[ln], ACT.Square).then_inc(sqhi_done[ln], 1)

            def split_x(r, t):
                act.wait_ge(x_in[r.p], r.pair(16, 16))
                if t != 0:
                    act.wait_ge(var_done[1], r.count(1))
                nc.scalar.copy(split[1][0], x_ring[:, bass.ds(slot4(r), 1), :].rearrange("c r n -> c (r n)")
                               ).then_inc(hi_done[1], 1)

            def log(r, ln, first):
                act.wait_ge(var_done[ln], r.count(1, 1))
                if not first:
                    act.wait_ge(norm_done[ln], r.count(1))
                nc.scalar.activation(rs[ln], var_ps[ln][:, :], ACT.Ln, bias=eps[ln]).then_inc(ln_done[ln], 1)

            def root(r, ln):
                act.wait_ge(ln_done[ln], r.count(1, 1))
                nc.scalar.activation(rs[ln], rs[ln], ACT.Exp, scale=-0.5).then_inc(exp_done[ln], 1)

            def root_squared(r, ln):
                act.wait_ge(exp_done[ln], r.count(1, 1))
                nc.scalar.activation(sq[ln], rs[ln], ACT.Square).then_inc(rsq_done[ln], 1)

            split_x(Row(0, 0), 0)

            def row(r, split1, ln1, gates, ln2, ffn, t):
                ahead, before, done = r + 2, r + -1, r + -2
                if ln2:
                    act.wait_ge(x1_done, before.count(2, 2))
                    if t is None or t >= 2:
                        act.wait_ge(var_done[2], before.count(1))
                    nc.scalar.copy(split[2][0], x1[before.p]).then_inc(hi_done[2], 1)
                if gates:
                    gate_g(r, 0, t)
                if ln1:
                    if t is None or t >= -1:
                        act.wait_ge(w_done[1], ahead.count(1))
                    squares(ahead, 1)
                if gates:
                    gate_i(r, 0)
                if ffn:
                    act.wait_ge(ffn_done, done.count(1, 1))
                    if t is None or t >= 4:
                        act.wait_ge(wx_out[done.p], done.pair(48))
                        act.wait_ge(bn_done, done.count(1, -1))
                    nc.scalar.activation(stage[done.p], q_ps[:, :], ACT.Copy, scale=unscale[:, 4:5]).then_inc(ev_done, 1)
                if ln2:
                    if t is None or t >= 2:
                        act.wait_ge(w_done[2], before.count(1))
                    squares(before, 2)
                if gates:
                    gate_f(r, 0)
                if split1:
                    split_x(r + 3, None if t is None else t + 3)
                if gates:
                    gate_c(r, 0)
                    gate_o(r, 0)
                if ln1 or ln2:
                    nc.scalar.preload_act_table_set("natural_log_exp_and_others")
                if ln1:
                    log(ahead, 1, t == -2)
                if gates:
                    gate_h(r, 0, t)
                if ln1:
                    root(ahead, 1)
                if ln2:
                    log(before, 2, t == 1)
                if ln1:
                    root_squared(ahead, 1)
                if ln2:
                    root(before, 2)
                    root_squared(before, 2)
                if gates:
                    nc.scalar.preload_act_table_set("sigmoid_and_others")
                    gate_g(r, 1, t)
                    gate_i(r, 1)
                    gate_f(r, 1)
                if ln1:
                    act.wait_ge(norm_done[1], ahead.count(1, 1))
                    if gates:
                        act.wait_ge(gate_done, r.count(8, 8))
                    nc.scalar.copy(xn[ahead.p][0][:, :, 1:W + 1], d[1].rearrange("c (b w) -> c b w", b=B)
                                   ).then_inc(nhi_done[1], 1)
                if gates:
                    gate_c(r, 1)
                    gate_o(r, 1)
                if ln2:
                    act.wait_ge(norm_done[2], before.count(1, 1))
                    if t is None or t >= 2:
                        act.wait_ge(ffn_done, before.count(1))
                    nc.scalar.copy(yn[0], d[2]).then_inc(nhi_done[2], 1)
                if gates:
                    gate_h(r, 1, t)

            def gate_g(r, g, t):
                act.wait_ge(gate_done, r.count(8, 4 * g + 1))
                if t != 0 or g:
                    act.wait_ge(c_done, r.count(2, g))
                nc.scalar.activation(gg, gate_ps[0][:, :], ACT.Tanh, bias=bias[:, 3:4], scale=unscale[:, 3:4]).then_inc(g_done, 1)

            def sigmoid(r, g, k, done):
                act.wait_ge(gate_done, r.count(8, 4 * g + k + 1))
                b = GATE_ROWS[k]
                nc.scalar.activation(gate_ps[k][:, :], gate_ps[k][:, :], ACT.Sigmoid, bias=bias[:, b:b + 1],
                                     scale=unscale[:, b:b + 1]).then_inc(done, 1)

            def gate_i(r, g):
                sigmoid(r, g, 1, i_done)

            def gate_f(r, g):
                sigmoid(r, g, 2, f_done)

            def gate_c(r, g):
                act.wait_ge(c_done, r.count(2, g + 1))
                nc.scalar.activation(hh[g], cell[g], ACT.Tanh).then_inc(tc_done, 1)

            def gate_o(r, g):
                sigmoid(r, g, 3, o_done)

            def gate_h(r, g, t):
                act.wait_ge(h_done, r.count(2, g + 1))
                nc.scalar.activation(hs[0][:, g * GB:(g + 1) * GB, 1:W + 1], hh[g].rearrange("c (b w) -> c b w", b=GB),
                                     ACT.Copy, scale=OPERAND_SCALE).then_inc(hhi_done, 1)

            rows(act, row)

            nc.scalar.preload_act_table_set("sigmoid_and_others")
            act.wait_ge(bn_ready, 1)
            for q in range(Q):
                if q == 0:
                    for p in range(2):
                        act.wait_ge(wx_out[p], 48 * H // 2)
                nc.scalar.activation(warm_columns(warm_y[0], q), warm_source(0, q), ACT.Sigmoid, bias=bn_b,
                                     scale=bn_s).then_inc(y_done[q], 1)
            for j in range(1, WARM):
                for q in range(Q):
                    act.wait_ge(z_done[q], j)
                    y = warm_columns(warm_y[j % 2], q)
                    nc.scalar.activation(y, z_ps[q][:, 0:y.shape[1]], ACT.Sigmoid, bias=bn_b).then_inc(y_done[q], 1)
            with act.Fori(0, SLICES) as ws:
                here = act.snap(slot_of(ws) * SLOT)
                for w in range(SW):
                    for q in range(Q):
                        act.wait_ge(z_done[q], ws * SW + (WARM + w))
                        nc.scalar.activation(columns(here, q, w), z_ps[q][:, 0:q_columns(q)], ACT.Sigmoid,
                                             bias=bn_b).then_inc(y_done[q], 1)
            act.wait_ge(flag_ready, 1)
            f = act.value_load(flag[0:1, 0:1])
            with act.If(f < 1):
                with act.Fori(0, H * SLICES) as n:
                    for w in range(SW):
                        act.wait_ge(ex_z, n * SW + (w + 1))
                        act.wait_ge(ex_add, n * SW + w)
                        nc.scalar.activation(ex_state, p_ps[:, 0:B], ACT.Sigmoid, bias=bn_b).then_inc(ex_y, 1)
            act.nop()

        @block.gpsimd
        def _(pool):
            def row(r, split1, ln1, gates, ln2, ffn, t):
                ahead, before = r + 2, r + -1
                if ln1:
                    squares_lo(pool, nc.gpsimd, ahead, 1)
                if t == -2:
                    pool.wait_ge(prep, 2)
                    nc.gpsimd.partition_all_reduce(most_all, most, C, bass.bass_isa.ReduceOp.max).then_inc(prep_pool, 1)
                    nc.gpsimd.partition_all_reduce(least_all, least, C, bass.bass_isa.ReduceOp.max).then_inc(prep_pool, 1)
                if ln2 and t != H:
                    squares_lo(pool, nc.gpsimd, before, 2)
                if ln1 and not dve_splits(t):
                    normed_x_lo(pool, nc.gpsimd, ahead)
                if ln2 and not dve_splits(t):
                    normed_x1_lo(pool, nc.gpsimd, before)

            rows(pool, row)

            pool.wait_ge(bn_step, 2)
            nc.gpsimd.tensor_tensor(bn_s, bn_t, half, ALU.pow).then_inc(bn_step, 1)

            for p in range(2):
                pool.wait_ge(x1_out[p], 32 * H // 2)
            for ws in range(SLICES):
                for q in range(Q):
                    pool.wait_ge(y_done[q], WARM + (ws + 1) * SW)
                if ws == RING - 1:
                    pool.wait_ge(slice_in, 16 * FIRST_KEPT)
                s = slot_of(ws)
                pool.dma_start(out_d[:, ws, :, :].rearrange("c h n -> c (h n)"), slices[:, s * SLOT:(s + 1) * SLOT],
                               accum_op=ALU.add, max_dma_last_dim=2048).then_inc(slice_out[ws], 16)
            for ws in range(SLICES):
                pool.wait_ge(slice_out[ws], 16)

        @block.vector
        def _(dve):
            def step(ins, sem_, count):
                ins.then_inc(sem_, 1)
                dve.wait_ge(sem_, count)

            nc.vector.memset(ones_bf, 1.0 / C)
            nc.vector.memset(eps[1], CONV_EPS)
            nc.vector.memset(eps[2], TOKEN_EPS)
            nc.vector.memset(half, -0.5)
            for r in range(2):
                for j in range(2):
                    nc.vector.memset(xn[r][j][:, :, 0:1], 0.0)
            for j in range(2):
                nc.vector.memset(hs[j][:, :, 0:1], 0.0)
                nc.vector.memset(hs[j][:, :, W + 1:W + 2], 0.0)
            for g in range(G):
                ins = nc.vector.memset(cell[g], 0.0)
            ins.then_inc(constants, 1)

            def measure_weights():
                dve.wait_ge(loaded, 16 * LOADS)
                by_gate = raw_c.rearrange("c k g o -> c g k o")
                nc.vector.tensor_reduce(most[:, 0:4], by_gate, AX.XY, ALU.max)
                nc.vector.tensor_reduce(least[:, 0:4], by_gate, AX.XY, ALU.min, negate=True)
                nc.vector.tensor_reduce(most[:, 4:5], raw_f, AX.X, ALU.max).then_inc(prep, 1)
                nc.vector.tensor_reduce(least[:, 4:5], raw_f, AX.X, ALU.min, negate=True).then_inc(prep, 1)

            def split_weights():
                nc.vector.tensor_tensor(bias, bias_is, bias_ss, ALU.add)
                dve.wait_ge(prep_pool, 2)
                step(nc.vector.tensor_tensor(most_all, most_all, least_all, ALU.max), prep, 3)
                step(nc.vector.tensor_scalar(most_all, most_all, 2.0 ** -60, None, ALU.max), prep, 4)
                step(nc.vector.tensor_scalar(most_all.bitcast(I32), most_all.bitcast(I32), 0x7F800000, None,
                                             ALU.bitwise_and), prep, 5)
                step(nc.vector.reciprocal(rescale, most_all), prep, 6)
                step(nc.vector.tensor_scalar(rescale, rescale, WEIGHT_SCALE, None, ALU.mult), prep, 7)
                nc.vector.tensor_scalar(unscale, most_all, 1.0 / (WEIGHT_SCALE * OPERAND_SCALE), None, ALU.mult)
                for g in range(4):
                    nc.vector.tensor_scalar(wc[0][:, :, g], raw_c[:, :, g], rescale[:, g:g + 1], None, ALU.mult)
                step(nc.vector.tensor_scalar(wf[0], raw_f, rescale[:, 4:5], None, ALU.mult), prep, 8)
                for g in range(4):
                    nc.vector.scalar_tensor_tensor(wc[1][:, :, g], raw_c[:, :, g], rescale[:, g:g + 1], wc[0][:, :, g],
                                                   ALU.mult, ALU.subtract)
                nc.vector.scalar_tensor_tensor(wf[1], raw_f, rescale[:, 4:5], wf[0], ALU.mult,
                                               ALU.subtract).then_inc(weights_ready, 1)

            def lo_part(r, ln, src):
                dve.wait_ge(hi_done[ln], r.count(1, 1))
                nc.vector.tensor_tensor(split[ln][1], src, split[ln][0], ALU.subtract).then_inc(lo_done[ln], 1)

            def centre(r, ln, src):
                dve.wait_ge(mean_done[ln], r.count(1, 1))
                nc.vector.tensor_tensor(d[ln], src, mean_ps[ln][:, :], ALU.subtract).then_inc(d_done[ln], 1)

            def sharpen(r, ln):
                dve.wait_ge(rsq_done[ln], r.count(1, 1))
                step(nc.vector.scalar_tensor_tensor(sq[ln], var_ps[ln][:, :], (0, CONV_EPS, TOKEN_EPS)[ln], sq[ln],
                                                    ALU.add, ALU.mult), u_done[ln], r.count(1, 1))
                nc.vector.scalar_tensor_tensor(rs[ln], sq[ln], 3.0, rs[ln], ALU.subtract, ALU.mult).then_inc(w_done[ln], 1)

            def norm(r, ln):
                dve.wait_ge(w_done[ln], r.count(1, 1))
                nc.vector.scalar_tensor_tensor(d[ln], rs[ln], -0.5 * OPERAND_SCALE, d[ln], ALU.mult,
                                               ALU.mult).then_inc(norm_done[ln], 1)

            def x_of(r):
                return x_ring[:, bass.ds(slot4(r), 1), :].rearrange("c r n -> c (r n)")

            def gate_i(r, g):
                dve.wait_ge(i_done, r.count(2, g + 1))
                nc.vector.tensor_tensor(gg, gate_ps[1][:, :], gg, ALU.mult).then_inc(ig_done, 1)

            def gate_f(r, g):
                dve.wait_ge(f_done, r.count(2, g + 1))
                dve.wait_ge(ig_done, r.count(2, g + 1))
                step(nc.vector.tensor_tensor(cell[g], gate_ps[2][:, :], cell[g], ALU.mult), fc_done, r.count(2, g + 1))
                nc.vector.tensor_tensor(cell[g], cell[g], gg, ALU.add).then_inc(c_done, 1)

            def gate_o(r, g, t):
                dve.wait_ge(o_done, r.count(2, g + 1))
                step(nc.vector.tensor_tensor(hh[g], gate_ps[3][:, :], hh[g], ALU.mult), h_done, r.count(2, g + 1))
                if t is None or t >= 2:
                    dve.wait_ge(x1_out[r.p], r.pair(32))
                dst = x1[r.p].rearrange("c (s b w) -> c s b w", s=SLICES, b=B)[:, :, g * GB:(g + 1) * GB, :]
                src = x_ring[:, bass.ds(slot4(r), 1), g * N:(g + 1) * N].rearrange("c r (b s w) -> c s (r b) w", b=GB, s=SLICES)
                nc.vector.tensor_tensor(dst, hh[g].rearrange("c (b s w) -> c s b w", b=GB, s=SLICES), src,
                                        ALU.add).then_inc(x1_done, 1)
                dve.wait_ge(hhi_done, r.count(2, g + 1))
                own = slice(g * GB, (g + 1) * GB)
                nc.vector.scalar_tensor_tensor(hs[1][:, own, 1:W + 1], hh[g].rearrange("c (b w) -> c b w", b=GB),
                                               OPERAND_SCALE, hs[0][:, own, 1:W + 1], ALU.mult,
                                               ALU.subtract).then_inc(hlo_done, 1)

            lo_part(Row(0, 0), 1, x_of(Row(0, 0)))

            def row(r, split1, ln1, gates, ln2, ffn, t):
                ahead, before, done = r + 2, r + -1, r + -2
                if ln1:
                    if t is None or t >= -1:
                        dve.wait_ge(nlo_done[1], ahead.count(1))
                    centre(ahead, 1, x_of(ahead))
                if t == -2:
                    measure_weights()
                if t == -1:
                    split_weights()
                if ln2:
                    lo_part(before, 2, x1[before.p])
                if gates:
                    gate_i(r, 0)
                if ln2:
                    if t is None or t >= 2:
                        dve.wait_ge(nlo_done[2], before.count(1))
                    centre(before, 2, x1[before.p])
                if gates:
                    gate_f(r, 0)
                if split1:
                    lo_part(r + 3, 1, x_of(r + 3))
                if ffn:
                    dve.wait_ge(ev_done, done.count(1, 1))
                    for b in range(2):
                        ins = nc.vector.bn_stats(bn_parts[:, bass.ds(done.count(2, b), 1), :],
                                                 stage[done.p][:, b * N:(b + 1) * N])
                    ins.then_inc(bn_done, 1)
                if gates:
                    gate_o(r, 0, t)
                if ln1:
                    sharpen(ahead, 1)
                    norm(ahead, 1)
                    if dve_splits(t):
                        normed_x_lo(dve, nc.vector, ahead)
                if ln2:
                    if t == H:
                        squares_lo(dve, nc.vector, before, 2)
                    sharpen(before, 2)
                if gates:
                    gate_i(r, 1)
                    gate_f(r, 1)
                if ln2:
                    norm(before, 2)
                    if dve_splits(t):
                        normed_x1_lo(dve, nc.vector, before)
                if gates:
                    gate_o(r, 1, t)

            rows(dve, row)

            dve.wait_ge(bn_done, H)
            step(nc.vector.bn_aggr(bn, bn_parts.rearrange("c r s -> c (r s)")), bn_step, 1)
            nc.vector.tensor_scalar(bn_t, bn[:, 1:2], BN_EPS, None, ALU.add).then_inc(bn_step, 1)
            dve.wait_ge(bn_step, 3)
            step(nc.vector.tensor_tensor(bn_s, bn_s, gamma, ALU.mult), bn_step, 4)
            step(nc.vector.tensor_tensor(bn_t, bn[:, 0:1], bn_s, ALU.mult), bn_step, 5)
            nc.vector.tensor_tensor(bn_b, beta, bn_t, ALU.subtract)
            for j in range(2):
                nc.vector.memset(warm_y[j][:, 0:B], 0.0)
            nc.vector.memset(ones_f, 1.0).then_inc(bn_ready, 1)

            def z(q, wx):
                out = z_ps[q][:, 0:wx.shape[1]]
                nc.vector.scalar_tensor_tensor(out, wx, bn_s, out, ALU.mult, ALU.add).then_inc(z_done[q], 1)

            for j in range(1, WARM):
                for q in range(Q):
                    dve.wait_ge(vy_done[q], j)
                    z(q, warm_source(j, q))
            for first, last in ((0, FIRST_KEPT), (FIRST_KEPT, SLICES)):
                with dve.Fori(first, last) as ws:
                    here = dve.snap(slot_of(ws) * SLOT)
                    if last == FIRST_KEPT:
                        dve.wait_ge(slice_in, ws * 16 + 16)
                    for w in range(SW):
                        for q in range(Q):
                            dve.wait_ge(vy_done[q], ws * SW + (WARM + w))
                            z(q, columns(here, q, w))

            for q in range(Q):
                dve.wait_ge(y_done[q], WARM + W)
            ended = slices[:, bass.ds(slot_of(SLICES - 1) * SLOT + SW - 1, COMPARED, step=SW)]
            gap = warm_y[WARM % 2][:, 0:COMPARED]
            step(nc.vector.tensor_tensor(gap, warm_y[(WARM - 1) % 2][:, B:ROW], ended, ALU.subtract), cmp_step, 1)
            step(nc.vector.tensor_tensor(gap, gap, gap, ALU.mult), cmp_step, 2)
            nc.vector.tensor_scalar(gap, gap, TOLERANCE ** 2, None, ALU.is_le, ALU.add, accum_out=same).then_inc(cmp_step, 1)
            dve.wait_ge(cmp_sum, 1)
            want = float(COMPARED * C) if not force_exact else -1.0
            nc.vector.tensor_scalar(flag, p_ps[:, 0:1], want, None, ALU.is_equal).then_inc(flag_ready, 1)
            dve.wait_ge(flag_ready, 1)
            f = dve.value_load(flag[0:1, 0:1])
            with dve.If(f < 1):
                nc.vector.memset(ex_state, 0.0).then_inc(ex_y, 1)
                with dve.Fori(0, H * SLICES) as n:
                    ws = dve.snap(n % SLICES)
                    dve.wait_ge(ex_in, n // SLICES * 32 + 32)
                    for w in range(SW):
                        dve.wait_ge(ex_vy, n * SW + (w + 1))
                        own = bass.ds(ws * SC + w, B, step=SW)
                        nc.vector.scalar_tensor_tensor(p_ps[:, 0:B], slices[:, own], bn_s, p_ps[:, 0:B], ALU.mult,
                                                       ALU.add).then_inc(ex_z, 1)
                        dve.wait_ge(ex_y, n * SW + (w + 2))
                        add = slices[:, bass.ds(ws * SC + (ROW + w), B, step=SW)]
                        nc.vector.tensor_tensor(add, add, ex_state, ALU.add).then_inc(ex_add, 1)
            dve.nop()


_OUT = (C, SLICES, H, B, SW)


def kernel(x, L0_conv_W_is, L0_conv_b_is, L0_conv_W_ss, L0_conv_b_ss, L0_ffn_W, L0_ffn_V, L0_ffn_gamma, L0_ffn_beta):
    import numpy as np
    import concourse.bacc as bacc
    from concourse.bass_utils import run_bass_kernel_spmd

    def taps(w, n):
        return np.asarray(w)[:, :, 0, :n].reshape(4, C, C, n).transpose(2, 3, 0, 1)

    arrays = {
        "x": np.asarray(x).transpose(1, 2, 0, 3).reshape(C, H, ROW),
        "w_is": taps(L0_conv_W_is, XT), "w_ss": taps(L0_conv_W_ss, HT),
        "b_is": np.asarray(L0_conv_b_is).reshape(4, C).T, "b_ss": np.asarray(L0_conv_b_ss).reshape(4, C).T,
        "ffn_w": np.asarray(L0_ffn_W).T, "ffn_v": np.asarray(L0_ffn_V).T,
        "gamma": np.asarray(L0_ffn_gamma).reshape(C, 1), "beta": np.asarray(L0_ffn_beta).reshape(C, 1),
    }
    arrays = {k: np.ascontiguousarray(v) for k, v in arrays.items()}
    nc = bacc.Bacc("TRN2", target_bir_lowering=False, num_devices=1)
    args = [nc.dram_tensor(k, v.shape, mybir.dt.from_np(v.dtype), kind="ExternalInput").ap() for k, v in arrays.items()]
    out = nc.dram_tensor("out", (C, SLICES, H, SC), F32, kind="ExternalOutput").ap()
    build(nc, *args, out)
    r = run_bass_kernel_spmd(nc, [arrays], core_ids=[0])
    return r.results[0]["out"].reshape(_OUT).transpose(3, 0, 2, 1, 4).reshape(B, C, H, W)
```
